# Optimizing a Trainium2 kernel written in Bass

```python
import numpy as np
import jax
import jax.numpy as jnp

def _softmax(x, axis=-1):
    return jax.nn.softmax(x, axis=axis)

def _gelu(x):
    return jax.nn.gelu(x, approximate=True)

def _silu(x):
    return jax.nn.silu(x)

def _sigmoid(x):
    return jax.nn.sigmoid(x)

def _layernorm(x, axis=-1, eps=1e-05):
    m = jnp.mean(x, axis=axis, keepdims=True)
    v = jnp.var(x, axis=axis, keepdims=True)
    return (x - m) / jnp.sqrt(v + eps)

def _scatter_add(tgt, idx, src, axis=0):
    return tgt.at[idx].add(src)

def _segment_sum(src, seg, n):
    return jax.ops.segment_sum(src, seg, n)
kernel_name = 'mk_xattn_seq_d2_seqx_r8_a01c1d'

def setup_inputs(seed: int=0):
    np.random.seed(seed)
    _w = jnp.asarray

    def _rec_inputs():
        import jax
        import jax.numpy as jnp
        _rk = jax.random.key(seed)
        x = -0.0001661 + 0.9999 * jax.random.normal(jax.random.fold_in(_rk, 1), (2, 512, 128), jnp.float32)
        _lenS = 512 - jax.random.randint(jax.random.fold_in(_rk, 7), (2,), 0, max(1, 512 // 4) + 1, jnp.int32)
        _lenS2 = 154 - jax.random.randint(jax.random.fold_in(_rk, 8), (2,), 0, max(1, 154 // 4) + 1, jnp.int32)
        _ctx_768P = jax.random.normal(jax.random.fold_in(_rk, 11), (2, 16, 96), jnp.float32)
        _ctx_768c = jax.random.dirichlet(jax.random.fold_in(_rk, 511), 0.3 * jnp.ones((16,), jnp.float32), (2, 154))
        _ctx_768t = jnp.einsum('bsk,bkd->bsd', _ctx_768c, _ctx_768P)
        _ctx_768t = _ctx_768t * jax.lax.rsqrt(jnp.mean(jnp.square(_ctx_768t)) + 1e-12) * 0.953939
        ctx_768 = 8.47981e-05 + 1.00068 * (_ctx_768t + 0.3 * jax.random.normal(jax.random.fold_in(_rk, 611), (2, 154, 96), jnp.float32))
        return (x, ctx_768)
    x, ctx_768 = _rec_inputs()

    def _L0_xattn_setup():
        import jax, jax.numpy as jnp
        import numpy as np
        LATENT = 128
        TEXT = 96
        HEADS = 16
        HEAD_DIM = LATENT // HEADS
        SCALE = HEAD_DIM ** (-0.5)
        LN_EPS = 1e-05
        key = jax.random.key(seed)
        ks = jax.random.split(key, 16)
        B, Tx, Txf = (4, 512, 32)

        def lin(k, fan_in, fan_out):
            bound = 1.0 / np.sqrt(fan_in)
            kw, kb = jax.random.split(k)
            W = jax.random.uniform(kw, (fan_in, fan_out), jnp.float32, -bound, bound)
            b = jax.random.uniform(kb, (fan_out,), jnp.float32, -bound, bound)
            return (W, b)
        Wq, bq = lin(ks[0], LATENT, LATENT)
        Wk, bk = lin(ks[1], TEXT, LATENT)
        Wv, bv = lin(ks[2], TEXT, LATENT)
        Wo, bo = lin(ks[3], LATENT, LATENT)
        W1, b1 = lin(ks[4], LATENT, 4 * LATENT)
        W2, b2 = lin(ks[5], 4 * LATENT, LATENT)
        return {'x': jax.random.normal(ks[6], (B, Tx, LATENT), jnp.float32), 'xf': jax.random.normal(ks[7], (B, Txf, TEXT), jnp.float32), 'Wq': Wq, 'bq': bq, 'Wk': Wk, 'bk': bk, 'Wv': Wv, 'bv': bv, 'Wo': Wo, 'bo': bo, 'ln_g': jnp.ones((LATENT,), jnp.float32), 'ln_b': jnp.zeros((LATENT,), jnp.float32), 'W1': W1, 'b1': b1, 'W2': W2, 'b2': b2}
    _L0_xattn_all = _L0_xattn_setup()
    _L0_xattn_in = {k: v for k, v in _L0_xattn_all.items() if k in ('Wq', 'bq', 'Wk', 'bk', 'Wv', 'bv', 'Wo', 'bo', 'ln_g', 'ln_b', 'W1', 'b1', 'W2', 'b2')}
    del _L0_xattn_all

    def _L1_xattn_setup():
        import jax, jax.numpy as jnp
        import numpy as np
        HEADS = 16
        D_HEAD = 64
        EPS = 1e-05

        def _ln(x, g, b):
            m = jnp.mean(x, axis=-1, keepdims=True)
            v = jnp.var(x, axis=-1, keepdims=True)
            return (x - m) * jax.lax.rsqrt(v + EPS) * g + b

        def _attn(xq, xc, Wq, Wk, Wv, Wo, bo):
            B, N, _ = xq.shape
            S = xc.shape[1]
            q = (xq @ Wq).reshape(B, N, HEADS, D_HEAD)
            k = (xc @ Wk).reshape(B, S, HEADS, D_HEAD)
            v = (xc @ Wv).reshape(B, S, HEADS, D_HEAD)
            scale = D_HEAD ** (-0.5)
            scores = jnp.einsum('bnhd,bshd->bhns', q, k) * scale
            attn = jax.nn.softmax(scores, axis=-1)
            out = jnp.einsum('bhns,bshd->bnhd', attn, v).reshape(B, N, HEADS * D_HEAD)
            return out @ Wo + bo

        def _geglu_ff(x, Wp, bp, Wf, bf):
            h = x @ Wp + bp
            a, gate = jnp.split(h, 2, axis=-1)
            return a * jax.nn.gelu(gate, approximate=False) @ Wf + bf
        key = jax.random.key(seed)
        ks = jax.random.split(key, 16)
        dim, ctx, inner, ffin = (128, 96, HEADS * D_HEAD, 4 * 128)

        def w(k, i, o):
            return jax.random.normal(k, (i, o), jnp.float32) * i ** (-0.5)
        inp = {'x': jax.random.normal(ks[0], (4, 256, dim), jnp.float32), 'context': jax.random.normal(ks[1], (4, 77, ctx), jnp.float32), 'Wq1': w(ks[2], dim, inner), 'Wk1': w(ks[3], dim, inner), 'Wv1': w(ks[4], dim, inner), 'Wo1': w(ks[5], inner, dim), 'bo1': jnp.zeros((dim,), jnp.float32), 'Wq2': w(ks[6], dim, inner), 'Wk2': w(ks[7], ctx, inner), 'Wv2': w(ks[8], ctx, inner), 'Wo2': w(ks[9], inner, dim), 'bo2': jnp.zeros((dim,), jnp.float32), 'Wp': w(ks[10], dim, 2 * ffin), 'bp': jnp.zeros((2 * ffin,), jnp.float32), 'Wf': w(ks[11], ffin, dim), 'bf': jnp.zeros((dim,), jnp.float32), 'g1': jnp.ones((dim,), jnp.float32), 'b1': jnp.zeros((dim,), jnp.float32), 'g2': jnp.ones((dim,), jnp.float32), 'b2': jnp.zeros((dim,), jnp.float32), 'g3': jnp.ones((dim,), jnp.float32), 'b3': jnp.zeros((dim,), jnp.float32)}
        return inp
    _L1_xattn_all = _L1_xattn_setup()
    _L1_xattn_in = {k: v for k, v in _L1_xattn_all.items() if k in ('Wq1', 'Wk1', 'Wv1', 'Wo1', 'bo1', 'Wq2', 'Wk2', 'Wv2', 'Wo2', 'bo2', 'Wp', 'bp', 'Wf', 'bf', 'g1', 'b1', 'g2', 'b2', 'g3', 'b3')}
    del _L1_xattn_all
    return {'x': x, 'ctx_768': ctx_768, 'L0_xattn_Wq': _L0_xattn_in['Wq'], 'L0_xattn_bq': _L0_xattn_in['bq'], 'L0_xattn_Wk': _L0_xattn_in['Wk'], 'L0_xattn_bk': _L0_xattn_in['bk'], 'L0_xattn_Wv': _L0_xattn_in['Wv'], 'L0_xattn_bv': _L0_xattn_in['bv'], 'L0_xattn_Wo': _L0_xattn_in['Wo'], 'L0_xattn_bo': _L0_xattn_in['bo'], 'L0_xattn_ln_g': _L0_xattn_in['ln_g'], 'L0_xattn_ln_b': _L0_xattn_in['ln_b'], 'L0_xattn_W1': _L0_xattn_in['W1'], 'L0_xattn_b1': _L0_xattn_in['b1'], 'L0_xattn_W2': _L0_xattn_in['W2'], 'L0_xattn_b2': _L0_xattn_in['b2'], 'L1_xattn_Wq1': _L1_xattn_in['Wq1'], 'L1_xattn_Wk1': _L1_xattn_in['Wk1'], 'L1_xattn_Wv1': _L1_xattn_in['Wv1'], 'L1_xattn_Wo1': _L1_xattn_in['Wo1'], 'L1_xattn_bo1': _L1_xattn_in['bo1'], 'L1_xattn_Wq2': _L1_xattn_in['Wq2'], 'L1_xattn_Wk2': _L1_xattn_in['Wk2'], 'L1_xattn_Wv2': _L1_xattn_in['Wv2'], 'L1_xattn_Wo2': _L1_xattn_in['Wo2'], 'L1_xattn_bo2': _L1_xattn_in['bo2'], 'L1_xattn_Wp': _L1_xattn_in['Wp'], 'L1_xattn_bp': _L1_xattn_in['bp'], 'L1_xattn_Wf': _L1_xattn_in['Wf'], 'L1_xattn_bf': _L1_xattn_in['bf'], 'L1_xattn_g1': _L1_xattn_in['g1'], 'L1_xattn_b1': _L1_xattn_in['b1'], 'L1_xattn_g2': _L1_xattn_in['g2'], 'L1_xattn_b2': _L1_xattn_in['b2'], 'L1_xattn_g3': _L1_xattn_in['g3'], 'L1_xattn_b3': _L1_xattn_in['b3']}

def reference(x, ctx_768, L0_xattn_Wq, L0_xattn_bq, L0_xattn_Wk, L0_xattn_bk, L0_xattn_Wv, L0_xattn_bv, L0_xattn_Wo, L0_xattn_bo, L0_xattn_ln_g, L0_xattn_ln_b, L0_xattn_W1, L0_xattn_b1, L0_xattn_W2, L0_xattn_b2, L1_xattn_Wq1, L1_xattn_Wk1, L1_xattn_Wv1, L1_xattn_Wo1, L1_xattn_bo1, L1_xattn_Wq2, L1_xattn_Wk2, L1_xattn_Wv2, L1_xattn_Wo2, L1_xattn_bo2, L1_xattn_Wp, L1_xattn_bp, L1_xattn_Wf, L1_xattn_bf, L1_xattn_g1, L1_xattn_b1, L1_xattn_g2, L1_xattn_b2, L1_xattn_g3, L1_xattn_b3):
    import jax
    import jax.numpy as jnp

    def _L0_xattn_ref(x, xf, Wq, bq, Wk, bk, Wv, bv, Wo, bo, ln_g, ln_b, W1, b1, W2, b2):
        import jax, jax.numpy as jnp
        import numpy as np
        LATENT = 128
        TEXT = 96
        HEADS = 16
        HEAD_DIM = LATENT // HEADS
        SCALE = HEAD_DIM ** (-0.5)
        LN_EPS = 1e-05
        B, Tx, D = x.shape
        Txf = xf.shape[1]
        q = (x @ Wq + bq).reshape(B, Tx, HEADS, HEAD_DIM).transpose(0, 2, 1, 3)
        k = (xf @ Wk + bk).reshape(B, Txf, HEADS, HEAD_DIM).transpose(0, 2, 1, 3)
        v = (xf @ Wv + bv).reshape(B, Txf, HEADS, HEAD_DIM).transpose(0, 2, 1, 3)
        scores = jnp.einsum('bhqd,bhkd->bhqk', q * SCALE, k)
        probs = jax.nn.softmax(scores, axis=-1)
        attn = jnp.einsum('bhqk,bhkd->bhqd', probs, v)
        out = attn.transpose(0, 2, 1, 3).reshape(B, Tx, D)
        out = out @ Wo + bo
        mu = jnp.mean(out, axis=-1, keepdims=True)
        var = jnp.var(out, axis=-1, keepdims=True)
        h = (out - mu) * jax.lax.rsqrt(var + LN_EPS) * ln_g + ln_b
        h = jax.nn.gelu(h @ W1 + b1, approximate=False)
        ffn = h @ W2 + b2
        out = out + ffn
        return x + out

    def _L1_xattn_ref(x, context, Wq1, Wk1, Wv1, Wo1, bo1, Wq2, Wk2, Wv2, Wo2, bo2, Wp, bp, Wf, bf, g1, b1, g2, b2, g3, b3):
        import jax, jax.numpy as jnp
        import numpy as np
        HEADS = 16
        D_HEAD = 64
        EPS = 1e-05

        def _ln(x, g, b):
            m = jnp.mean(x, axis=-1, keepdims=True)
            v = jnp.var(x, axis=-1, keepdims=True)
            return (x - m) * jax.lax.rsqrt(v + EPS) * g + b

        def _attn(xq, xc, Wq, Wk, Wv, Wo, bo):
            B, N, _ = xq.shape
            S = xc.shape[1]
            q = (xq @ Wq).reshape(B, N, HEADS, D_HEAD)
            k = (xc @ Wk).reshape(B, S, HEADS, D_HEAD)
            v = (xc @ Wv).reshape(B, S, HEADS, D_HEAD)
            scale = D_HEAD ** (-0.5)
            scores = jnp.einsum('bnhd,bshd->bhns', q, k) * scale
            attn = jax.nn.softmax(scores, axis=-1)
            out = jnp.einsum('bhns,bshd->bnhd', attn, v).reshape(B, N, HEADS * D_HEAD)
            return out @ Wo + bo

        def _geglu_ff(x, Wp, bp, Wf, bf):
            h = x @ Wp + bp
            a, gate = jnp.split(h, 2, axis=-1)
            return a * jax.nn.gelu(gate, approximate=False) @ Wf + bf
        x = _attn(_ln(x, g1, b1), _ln(x, g1, b1), Wq1, Wk1, Wv1, Wo1, bo1) + x
        x = _attn(_ln(x, g2, b2), context, Wq2, Wk2, Wv2, Wo2, bo2) + x
        x = _geglu_ff(_ln(x, g3, b3), Wp, bp, Wf, bf) + x
        return x
    x = _L0_xattn_ref(x, ctx_768, L0_xattn_Wq, L0_xattn_bq, L0_xattn_Wk, L0_xattn_bk, L0_xattn_Wv, L0_xattn_bv, L0_xattn_Wo, L0_xattn_bo, L0_xattn_ln_g, L0_xattn_ln_b, L0_xattn_W1, L0_xattn_b1, L0_xattn_W2, L0_xattn_b2)
    x = _L1_xattn_ref(x, ctx_768, L1_xattn_Wq1, L1_xattn_Wk1, L1_xattn_Wv1, L1_xattn_Wo1, L1_xattn_bo1, L1_xattn_Wq2, L1_xattn_Wk2, L1_xattn_Wv2, L1_xattn_Wo2, L1_xattn_bo2, L1_xattn_Wp, L1_xattn_bp, L1_xattn_Wf, L1_xattn_bf, L1_xattn_g1, L1_xattn_b1, L1_xattn_g2, L1_xattn_b2, L1_xattn_g3, L1_xattn_b3)
    return x

_drawn_inputs = setup_inputs


def setup_inputs(seed=0):
    import zlib

    import numpy as np

    out = dict(_drawn_inputs(seed))
    spreads = {'L0_xattn_ln_g': (1.0, 0.2),
     'L0_xattn_ln_b': (0.0, 0.338),
     'L1_xattn_bo1': (0.0, 0.1),
     'L1_xattn_bo2': (0.0, 0.1),
     'L1_xattn_bp': (0.0, 0.1),
     'L1_xattn_bf': (0.0, 0.1),
     'L1_xattn_g1': (1.0, 0.2),
     'L1_xattn_b1': (0.0, 0.1),
     'L1_xattn_g2': (1.0, 0.2),
     'L1_xattn_b2': (0.0, 0.348),
     'L1_xattn_g3': (1.0, 0.2),
     'L1_xattn_b3': (0.0, 0.1)}
    factors = {'L0_xattn_bq': 8.0, 'L0_xattn_bk': 8.0, 'L0_xattn_b1': 2.734}
    for name, (base, spread) in spreads.items():
        noise = np.random.default_rng([zlib.crc32(name.encode()), seed]).standard_normal(out[name].shape)
        drawn = base * np.exp(spread * noise) if base else spread * noise
        out[name] = jnp.asarray(drawn.astype(out[name].dtype))
    for name, factor in factors.items():
        out[name] = (out[name] * factor).astype(out[name].dtype)
    return out
```

```python
from contextlib import ExitStack

import concourse.bass as bass
from concourse import mybir

P = 128
D = 128
B = 2
N = 512
NT = B * N // P
TB = N // P
C = 96
S = 154
SC = S // 2
H = 16
HD0 = D // H
HD = 64
INNER = H * HD
FF = 4 * D
EPS = 1e-5
NPAIR = B * H // 2
PAIRS = H // 2
NQUAD = B * 4

F32 = mybir.dt.float32
F32R = mybir.dt.float32r
ALU = mybir.AluOpType
ACT = mybir.ActivationFunctionType
AX = mybir.AxisListType.X

COL = dict(bq0=0, bk0=4, nq0=8, nk0=9, ln_g=10, ln_b=11, b1=12, g1=16, c1=17, g2=18, c2=19, g3=20, c3=21, bp=22)
NCOL = 30
ROW = dict(bv0=0, bo0=1, b20=2, bo1=3, bo2=4, bf=5)


def build(nc, a, out):
    ctx = ExitStack()
    with ctx:
        def sb(name, shape, dt=F32):
            return ctx.enter_context(nc.sbuf_tensor(name, shape, dt))

        def sem(name):
            return ctx.enter_context(nc.semaphore(name))

        cols = sb("cols", [P, NCOL])
        rows = sb("rows", [P, len(ROW), D])
        ident = sb("ident", [P, P])
        ones = sb("ones", [P, HD])
        ctxT = sb("ctxT", [C, B * S])
        X = sb("X", [P, NT, D])
        O = sb("O", [P, NT, D])
        XC = sb("XC", [P, NT, D])
        xnT = sb("xnT", [P, B * N])
        Wq = sb("Wq", [D, INNER])
        Wk = sb("Wk", [D, INNER])
        Wv = sb("Wv", [D, INNER])
        Wo = sb("Wo", [P, PAIRS, D])
        w1 = sb("w1", [D, FF])
        w2 = sb("w2", [P, 4, D])
        wp = sb("wp", [D, 2 * FF])
        wf = sb("wf", [P, 4, D])
        R = sb("R", [P, 3, 4, 2, N], F32R)
        PT = sb("PT", [P, 2, 8, N])
        V = sb("V", [P, NT, INNER])
        AT = sb("AT", [P, 8, B * N])
        psums = sb("psums", [P, 2, N])
        mx0 = sb("mx0", [P, B, TB, H])
        mx = sb("mx", [P, 2, TB, 2])
        mneg = sb("mneg", [H, 2, N], F32R)
        st6 = sb("st6", [P, TB, 6])
        mv = sb("mv", [P, TB, 2])
        rstd = sb("rstd", [P, TB, 1])
        pvs = sb("pvs", [P, N])
        work = sb("work", [P, 2, N])
        lnv = sb("lnv", [P, TB, 1])

        Rflat = R[:, :, :, :, :].rearrange("p a b c n -> p (a b c n)")
        Q0 = Rflat[:, 0:4 * B * N].rearrange("p (t n) -> p t n", t=4)
        K0 = Rflat[:, 4096:4096 + 4 * B * S].rearrange("p (t n) -> p t n", t=4)
        half0 = Rflat[:, 6144:8192].rearrange("p (u n) -> p u n", u=2)
        PTflat = PT[:, :, :, :].rearrange("p a b n -> p (a b n)")
        full0 = PTflat[:, 0:2048].rearrange("p (u n) -> p u n", u=2)
        Vflat = V[:, :, :].rearrange("p t n -> p (t n)")
        V0 = Vflat[0:SC, 0:2048].rearrange("p (c h e) -> p c h e", c=4, h=H)
        wq0 = Vflat[:, 2048:2560].rearrange("p (t n) -> p t n", t=4)
        wk0 = Vflat[0:C, 2560:3072].rearrange("p (t n) -> p t n", t=4)
        wo0 = Vflat[:, 3072:3584].rearrange("p (t n) -> p t n", t=4)
        wv0 = Vflat[0:C, 3584:3712]
        PT0 = PT[:, :, :, :].rearrange("p a (j c) n -> p a j c n", c=2)
        PT1 = PT[:, :, :, :].rearrange("p a (h c) n -> p a h c n", c=4)

        ST = [ctx.enter_context(nc.psum_tensor(f"ST{i}", [P, 2, N], F32)) for i in range(2)]
        PV = ctx.enter_context(nc.psum_tensor("PV", [P, N], F32))
        DEN = ctx.enter_context(nc.psum_tensor("DEN", [P, N], F32))
        M = [ctx.enter_context(nc.psum_tensor(f"M{i}", [P, N], F32)) for i in range(2)]

        ld = {k: sem(f"ld_{k}") for k in ("xT", "wq0", "wk0", "ctxT", "wv0", "cols", "rows", "x", "ident", "wo0",
                                          "w1", "w2", "wq1", "wk1", "wv1", "wo1", "wq2", "wk2", "wv2", "wo2", "wp", "wf")}
        q0_done = sem("q0_done")
        full_done = sem("full_done")
        half_done = sem("half_done")
        split_done = sem("split_done")
        v0_done = sem("v0_done")
        v0_ready = sem("v0_ready")
        v0_zero = sem("v0_zero")
        ones_set = sem("ones_set")
        kones_set = sem("kones_set")
        m_full = sem("m_full")
        m_free = sem("m_free")
        mrow0 = sem("mrow0")
        st0_done = sem("st0_done")
        exp0_done = sem("exp0_done")
        pv0_done = sem("pv0_done")
        rinv0_done = sem("rinv0_done")
        norm0_done = sem("norm0_done")

        class Phase:
            def __init__(self, name, rows_of_chunk, chunks):
                self.KC, self.NC = rows_of_chunk, chunks
                self.NK = rows_of_chunk * chunks
                self.units = chunks
                self.name = name
                self.proj = sem(f"{name}_proj")
                self.hi = sem(f"{name}_hi")
                self.lo = sem(f"{name}_lo")
                self.mrow = sem(f"{name}_mrow")
                self.st = sem(f"{name}_st")
                self.exp = sem(f"{name}_exp")
                self.sum = sem(f"{name}_sum")
                self.pv = sem(f"{name}_pv")
                self.pvs = sem(f"{name}_pvs")
                self.rinv = sem(f"{name}_rinv")
                self.den = sem(f"{name}_den")
                self.norm = sem(f"{name}_norm")
                self.smax = 2 * TB if chunks == 4 else TB

        self_att = Phase("self", P, 4)
        cross_att = Phase("cross", SC, 2)

        o_done = [sem(f"o_done{i}") for i in range(3)]
        xc_done = [sem(f"xc_done{i}") for i in range(4)]
        t_done = [sem(f"t_done{i}") for i in range(4)]
        xn_done = [sem(f"xn_done{i}") for i in range(4)]
        o_read = [sem(f"o_read{i}") for i in range(3)]
        w1_done = sem("w1_done")
        gelu_done = sem("gelu_done")
        w2_done = sem("w2_done")
        w2_read = sem("w2_read")
        v_done = [sem("v1_done"), sem("v2_done")]
        va_done = [sem("v1a_done"), sem("v2a_done")]
        vd_done = [sem("v1d_done"), sem("v2d_done")]
        wp_done = sem("wp_done")
        gate_done = sem("gate_done")
        glu_done = sem("glu_done")
        wf_done = sem("wf_done")
        y_done = sem("y_done")
        stored = sem("stored")
        var_done = [sem(f"var_done{i}") for i in range(4)]
        rs_done = [sem(f"rs_done{i}") for i in range(4)]
        act_step = sem("act_step")
        dve_step = sem("dve_step")
        pool_step = sem("pool_step")

        units, freed = [], {}

        def unit(key, semaphore, count):
            freed[key] = (semaphore, count)
            units.append(key)

        for n in range(6):
            unit(("q0", n), full_done, n + 1)
        unit(("v0",), v0_ready, 1)
        for i in range(NQUAD):
            for j in range(4):
                unit(("s0", i, j), exp0_done, 4 * i + j + 1)

        def pair_units(ph):
            order = [("proj", 0), ("proj", 1)]
            for i in range(NPAIR):
                if i + 2 < NPAIR:
                    order.append(("proj", i + 2))
                order += [("st", i, n) for n in range(ph.units)]
            for key in order:
                if key[0] == "proj":
                    unit((ph.name,) + key, ph.lo, key[1] + 1)
                else:
                    unit((ph.name,) + key, ph.exp, key[1] * ph.units + key[2] + 1)

        unit(("o", 0), o_read[0], B)
        unit(("t", 0), xn_done[0], B)
        for n in range(B * 2):
            unit(("w1", n), gelu_done, 2 * (n + 1))
        unit(("w2",), w2_read, B)
        unit(("t", 1), xn_done[1], B)
        for t in range(NT):
            unit(("v", 0, t), (va_done if t % 2 == 0 else vd_done)[0], t // 2 + 1)
        pair_units(self_att)
        for t in range(4):
            unit(("v", 1, t), (va_done if t % 2 == 0 else vd_done)[1], t // 2 + 1)
        unit(("o", 1), o_read[1], B)
        unit(("t", 2), xn_done[2], B)
        pair_units(cross_att)
        unit(("o", 2), o_read[2], B)
        unit(("t", 3), xn_done[3], B)
        for n in range(B * 4):
            unit(("wp", n), glu_done, n + 1)
        unit(("wf",), y_done, B)
        place = {key: n for n, key in enumerate(units)}

        per_b = TB * H // 2
        turned = {("layer0", 0): per_b + 1, ("layer0", 1): 2 * per_b + 2}
        uses = 2 * per_b + 2
        for ph in (self_att, cross_att):
            for i in range(NPAIR):
                uses += ph.smax + 1
                turned[ph.name, i] = uses

        def bank(key):
            return ST[place[key] % 2]

        def reg(i, kind):
            return R[:, i % 3, ("AQ", "BQ", "AK", "BK").index(kind)]

        block = ctx.enter_context(nc.Block())

        @block.sync
        def _(sp):
            def load(key, dst, src):
                sp.dma_start(dst, src).then_inc(ld[key], 16)

            load("xT", xnT[:, :], a["xT"])
            load("wq0", wq0, a["wq0"])
            load("cols", cols[:, :], a["cols"])
            load("ctxT", ctxT[:, :], a["ctxT"])
            load("wk0", wk0, a["wk0"])
            load("wv0", wv0, a["wv0"])
            load("rows", rows[:, :, :], a["rows"])
            load("ident", ident[:, :], a["ident"])
            load("wo0", wo0, a["wo0"])
            load("x", X[:, :, :], a["x"].rearrange("b (t p) d -> p (b t) d", p=P))
            load("w1", w1[:, :], a["w1"])
            load("w2", w2[:, :, :], a["w2"].rearrange("(m p) d -> p m d", p=P))
            load("wv1", Wv[:, :], a["wv1"])
            load("wq1", Wq[:, :], a["wq1"])
            load("wk1", Wk[:, :], a["wk1"])
            load("wo1", Wo[:, :, :], a["wo1"].rearrange("(j p) d -> p j d", p=P))
            load("wp", wp[:, :], a["wp"])
            load("wf", wf[:, :, :], a["wf"].rearrange("(m p) d -> p m d", p=P))
            for b in range(B):
                sp.wait_ge(m_free, turned["layer0", b])
                for part in range(2):
                    for g in range(4):
                        sp.dma_start(Q0[32 * g + 24 + part:32 * g + 25 + part, :, b * N:(b + 1) * N].bitcast(F32),
                                     mneg[4 * g:4 * g + 4, part, :].bitcast(F32)).then_inc(mrow0, 16)

            def maxima_rows(ph):
                for i in range(NPAIR):
                    sp.wait_ge(m_free, turned[ph.name, i])
                    if i >= 3:
                        sp.wait_ge(ph.st, ph.units * (i - 2))
                    for part in range(2):
                        sp.dma_start(reg(i, "BQ")[HD + part:HD + part + 1, :, :].bitcast(F32),
                                     mneg[0:2, part, :].bitcast(F32)).then_inc(ph.mrow, 16)

            sp.wait_ge(kones_set, 1)
            maxima_rows(self_att)
            sp.wait_ge(self_att.proj, NPAIR)
            load("wv2", Wv[0:C, :], a["wv2"])
            load("wq2", Wq[:, :], a["wq2"])
            load("wk2", Wk[0:C, :], a["wk2"])
            sp.wait_ge(o_done[1], B)
            load("wo2", Wo[:, :, :], a["wo2"].rearrange("(j p) d -> p j d", p=P))
            maxima_rows(cross_att)
            y = out.rearrange("b (t p) d -> p b t d", p=P)
            for b in range(B):
                sp.wait_ge(y_done, b + 1)
                sp.dma_start(y[:, b], O[:, TB * b:TB * (b + 1), :]).then_inc(stored, 16)
            sp.wait_ge(stored, 16 * B)

        @block.gpsimd
        def _(pool):
            steps = [0]

            def link(ins):
                steps[0] += 1
                ins.then_inc(pool_step, 1)
                pool.wait_ge(pool_step, steps[0])

            pool.memset(ones[:, :], 1.0).then_inc(ones_set, 1)
            pool.memset(V0, 0.0).then_inc(v0_zero, 1)
            pool.wait_ge(pv0_done, NQUAD)
            for i in range(3):
                pool.memset(reg(i, "BQ")[HD:P, :, :].bitcast(F32), 0.0)
                link(pool.memset(reg(i, "BK")[HD:P, :, :].bitcast(F32), 0.0))
                ins = pool.memset(reg(i, "BK")[HD:HD + 2, :, :].bitcast(F32), 1.0)
            ins.then_inc(kones_set, 1)

            def sums(ph):
                for i in range(NPAIR):
                    pool.wait_ge(ph.exp, ph.units * (i + 1))
                    if i >= 1:
                        pool.wait_ge(ph.den, i)
                    p = PT1[0:ph.KC, i % 2]
                    s = psums[0:ph.KC, :, :]
                    ins = pool.tensor_tensor(s, p[:, :, 0, :], p[:, :, 1, :], ALU.add)
                    for c in range(2, ph.NC):
                        link(ins)
                        ins = pool.tensor_tensor(s, s, p[:, :, c, :], ALU.add)
                    ins.then_inc(ph.sum, 1)

            sums(self_att)
            sums(cross_att)

        @block.scalar
        def _(act):
            steps = [0]

            def link(ins):
                steps[0] += 1
                ins.then_inc(act_step, 1)
                act.wait_ge(act_step, steps[0])

            exp_ln = "natural_log_exp_and_others"
            act.preload_act_table_set(exp_ln)

            for n in range(6):
                act.wait_ge(full_done, n + 1)
                if n >= 2:
                    act.wait_ge(split_done, n - 1)
                w = B * N if n < 4 else 2 * B * S
                act.activation(half0[:, n % 2, 0:w], full0[:, n % 2, 0:w], ACT.Copy).then_inc(half_done, 1)

            def copy_pv(pv, norm, k):
                act.wait_ge(pv, k + 1)
                if k >= 1:
                    act.wait_ge(norm, k)
                return act.activation(pvs[:, :], PV[:, :], ACT.Copy, scale=-1.0)

            def invert(done):
                link(act.activation(work[:, 0, :], DEN[:, :], ACT.Ln))
                act.activation(work[:, 1, :], work[:, 0, :], ACT.Exp, scale=-1.0).then_inc(done, 1)

            for i in range(NQUAD + 1):
                for j in range(4 if i < NQUAD else 0):
                    act.wait_ge(st0_done, 4 * i + j + 1)
                    if i >= 2:
                        act.wait_ge(pv0_done, i - 1)
                    act.activation(PT0[0:SC, i % 2, j], bank(("s0", i, j))[0:SC, :, :], ACT.Exp).then_inc(exp0_done, 1)
                if i >= 1:
                    copy_pv(pv0_done, norm0_done, i - 1)
                    invert(rinv0_done)

            def gain_bias(n, g, c):
                for b in range(B):
                    act.wait_ge(var_done[n], b + 1)
                    link(act.activation(lnv[:, :, :], mv[:, :, 1:2], ACT.Ln))
                    act.activation(rstd[:, :, :], lnv[:, :, :], ACT.Exp, scale=-0.5).then_inc(rs_done[n], 1)
                    scale_features(n, g, c, b)

            def scale_features(n, g, c, b):
                act.wait_ge(t_done[n], b + 1)
                act.activation(xnT[:, b * N:(b + 1) * N], bank(("t", n))[:, b, :], ACT.Identity,
                               scale=cols[:, g:g + 1], bias=cols[:, c:c + 1]).then_inc(xn_done[n], 1)

            def values(n, tiles, r):
                for t in range(0, tiles, 2):
                    act.wait_ge(v_done[n], t + 1)
                    act.activation(V[0:r, t, :].rearrange("p (u n) -> p u n", u=2), bank(("v", n, t))[0:r],
                                   ACT.Copy).then_inc(va_done[n], 1)

            def halves(ph, i):
                act.wait_ge(ph.proj, i + 1)
                if i >= 3:
                    act.wait_ge(ph.st, ph.units * (i - 2))
                u = bank((ph.name, "proj", i))
                for kind, r0, src, w, scale in (("AQ", 0, 0, N, HD ** -0.5), ("AK", 0, 1, ph.NK, 1.0),
                                                ("BQ", 0, 0, N, HD ** -0.5), ("AK", HD, 1, ph.NK, 1.0)):
                    for h in range(2):
                        ins = act.activation(reg(i, kind)[r0:r0 + HD, h, 0:w], u[HD * h:HD * h + HD, src, 0:w],
                                             ACT.Copy, scale=scale)
                ins.then_inc(ph.hi, 1)

            def exponentials(ph, i):
                per = ph.units // 2
                for n in range(ph.units):
                    act.wait_ge(ph.st, ph.units * i + n + 1)
                    if i >= 2:
                        act.wait_ge(ph.pv, i - 1)
                        act.wait_ge(ph.sum, i - 1)
                    h, c = n // per, 2 * (n % per)
                    act.activation(PT1[0:ph.KC, i % 2, h, c:c + 2, :], bank((ph.name, "st", i, n))[0:ph.KC, :, :],
                                   ACT.Exp).then_inc(ph.exp, 1)

            def attention(ph):
                halves(ph, 0)
                halves(ph, 1)
                for i in range(NPAIR + 1):
                    if i + 2 < NPAIR:
                        halves(ph, i + 2)
                    if i >= 1:
                        copy_pv(ph.pv, ph.norm, i - 1).then_inc(ph.pvs, 1)
                    if i >= 1:
                        act.wait_ge(ph.den, i)
                        invert(ph.rinv)
                    if i < NPAIR:
                        exponentials(ph, i)

            gain_bias(0, COL["ln_g"], COL["ln_b"])
            for n in range(B * 2):
                act.wait_ge(w1_done, n + 1)
                b = n // 2
                for mm in range(2):
                    m = 2 * (n % 2) + mm
                    act.activation(AT[:, m, b * N:(b + 1) * N], bank(("w1", n))[:, mm, :], ACT.Gelu,
                                   bias=cols[:, COL["b1"] + m:COL["b1"] + m + 1]).then_inc(gelu_done, 1)
            act.preload_act_table_set(exp_ln)
            gain_bias(1, COL["g1"], COL["c1"])
            values(0, NT, P)
            act.wait_ge(kones_set, 1)
            attention(self_att)
            values(1, 4, SC)
            gain_bias(2, COL["g2"], COL["c2"])
            attention(cross_att)
            gain_bias(3, COL["g3"], COL["c3"])
            for n in range(B * 4):
                act.wait_ge(wp_done, n + 1)
                if n >= 2:
                    act.wait_ge(glu_done, n - 1)
                m = n % 4
                act.activation(work[:, n % 2, :], bank(("wp", n))[:, 0, :], ACT.Gelu,
                               bias=cols[:, COL["bp"] + 4 + m:COL["bp"] + 5 + m]).then_inc(gate_done, 1)

        @block.vector
        def _(dve):
            steps, ring = [0], [0]

            def link(ins):
                steps[0] += 1
                ins.then_inc(dve_step, 1)
                dve.wait_ge(dve_step, steps[0])

            def row(name):
                return rows[:, ROW[name], :]

            dve.wait_ge(ld["cols"], 16)

            def full(n):
                dve.wait_ge(q0_done, n + 1)
                if n >= 2:
                    dve.wait_ge(half_done, n - 1)
                    dve.wait_ge(split_done, n - 1)
                if n < 4:
                    dve.tensor_scalar(full0[:, n % 2, :], bank(("q0", n))[:, :, :].rearrange("p b n -> p (b n)"),
                                      cols[:, COL["bq0"] + n:COL["bq0"] + n + 1], HD0 ** -0.5,
                                      ALU.add, ALU.mult).then_inc(full_done, 1)
                else:
                    for u in range(2):
                        t = 2 * (n - 4) + u
                        ins = dve.tensor_scalar(full0[:, n % 2, u * B * S:(u + 1) * B * S], bank(("q0", n))[:, u, 0:B * S],
                                                cols[:, COL["bk0"] + t:COL["bk0"] + t + 1], None, ALU.add)
                    ins.then_inc(full_done, 1)

            def split(n):
                dve.wait_ge(half_done, n + 1)
                if n < 4:
                    w, dst, mask = B * N, Q0[:, n, :], COL["nq0"]
                else:
                    w, dst, mask = 2 * B * S, K0[:, 2 * (n - 4):2 * (n - 4) + 2, :].rearrange("p t n -> p (t n)"), COL["nk0"]
                dve.scalar_tensor_tensor(dst, half0[:, n % 2, 0:w].bitcast(F32), cols[:, mask:mask + 1],
                                         full0[:, n % 2, 0:w], ALU.mult, ALU.add).then_inc(split_done, 1)

            full(0)
            for n in range(6):
                if n + 1 < 6:
                    full(n + 1)
                split(n)
            dve.wait_ge(v0_done, 1)
            dve.wait_ge(v0_zero, 1)
            dve.wait_ge(ld["rows"], 16)
            for c in range(4):
                ins = dve.tensor_tensor(V0[:, c, :, 0:HD0],
                                        bank(("v0",))[0:SC, 0, c * D:(c + 1) * D].rearrange("p (h e) -> p h e", h=H),
                                        row("bv0")[0:SC].rearrange("p (h e) -> p h e", h=H), ALU.add)
            ins.then_inc(v0_ready, 1)
            dve.wait_ge(ld["x"], 16)
            for t in range(NT):
                ins = dve.tensor_tensor(X[:, t, :], X[:, t, :], row("b20"), ALU.add)
            link(ins)

            def take():
                k = ring[0]
                ring[0] += 1
                dve.wait_ge(m_full, k + 1)
                return M[k % 2]

            def maxima0(b, qt):
                for hp in range(H // 2):
                    dve.tensor_reduce(mx0[:, b, qt, 2 * hp:2 * hp + 2],
                                      take()[:, 0:2 * S].rearrange("p (h k) -> p h k", h=2), AX,
                                      ALU.max).then_inc(m_free, 1)

            for qt in range(TB):
                maxima0(0, qt)

            def negated(n):
                m = take()
                link(dve.tensor_scalar(mneg[0:n, 0, :], m[0:n, :], -1.0, None, ALU.mult))
                dve.scalar_tensor_tensor(mneg[0:n, 1, :], m[0:n, :], -1.0, mneg[0:n, 0, :].bitcast(F32),
                                         ALU.mult, ALU.subtract).then_inc(m_free, 1)

            def divide(dst, done):
                dve.tensor_tensor(pvs[:, :], pvs[:, :], work[:, 1, :], ALU.mult)
                link(dve.tensor_tensor(work[:, 0, :], DEN[:, :], work[:, 1, :], ALU.mult))
                dve.scalar_tensor_tensor(dst, work[:, 0, :], -2.0, pvs[:, :], ALU.add, ALU.mult).then_inc(done, 1)

            negated(H)
            for i in range(NQUAD + 1):
                if i < TB:
                    maxima0(1, i)
                if i == TB - 1:
                    dve.wait_ge(mrow0, 16 * 8)
                    negated(H)
                if i >= 1:
                    dve.wait_ge(rinv0_done, i)
                    b, t = (i - 1) // 4, (i - 1) % 4
                    divide(AT[:, 4 + t, b * N:(b + 1) * N], norm0_done)

            def layernorm(n, src, b):
                for t in range(TB):
                    ins = dve.bn_stats(st6[:, t, :], src[:, TB * b + t, :])
                link(ins)
                for t in range(TB):
                    ins = dve.bn_aggr(mv[:, t, :], st6[:, t, :])
                link(ins)
                v = mv[:, :, 1:2]
                dve.tensor_scalar(v, v, EPS, None, ALU.add).then_inc(var_done[n], 1)
                dve.wait_ge(rs_done[n], b + 1)
                link(dve.tensor_tensor(lnv[:, :, :], rstd[:, :, :], rstd[:, :, :], ALU.mult))
                link(dve.tensor_tensor(lnv[:, :, :], lnv[:, :, :], v, ALU.mult))
                link(dve.tensor_scalar(lnv[:, :, :], lnv[:, :, :], -0.5, 1.5, ALU.mult, ALU.add))
                link(dve.tensor_tensor(rstd[:, :, :], rstd[:, :, :], lnv[:, :, :], ALU.mult))
                for t in range(TB):
                    ins = dve.tensor_scalar(XC[:, TB * b + t, :], src[:, TB * b + t, :], mv[:, t, 0:1], rstd[:, t, 0:1],
                                            ALU.subtract, ALU.mult)
                ins.then_inc(xc_done[n], 1)

            def tiles(u, b):
                return bank(u)[:, b, :].rearrange("p (t d) -> p t d", t=TB)

            def add_row(dst, src, name, b):
                for t in range(TB):
                    ins = dve.tensor_tensor(dst[:, TB * b + t, :], src[:, t, :], row(name), ALU.add)
                return ins

            def half(b):
                return slice(TB * b, TB * (b + 1))

            for b in range(B):
                dve.wait_ge(o_done[0], b + 1)
                ins = add_row(O, tiles(("o", 0), b), "bo0", b)
                ins.then_inc(o_read[0], 1)
                dve.wait_ge(o_read[0], b + 1)
                layernorm(0, O, b)
            for b in range(B):
                dve.wait_ge(w2_done, b + 1)
                ins = dve.tensor_tensor(O[:, half(b), :], tiles(("w2",), b), O[:, half(b), :], ALU.add)
                ins.then_inc(w2_read, 1)
                dve.wait_ge(w2_read, b + 1)
                link(dve.tensor_tensor(X[:, half(b), :], O[:, half(b), :], X[:, half(b), :], ALU.add))
                layernorm(1, X, b)

            def values(n, tiles_, r):
                for t in range(1, tiles_, 2):
                    dve.wait_ge(v_done[n], t + 1)
                    dve.tensor_copy(V[0:r, t, :].rearrange("p (u n) -> p u n", u=2),
                                    bank(("v", n, t))[0:r]).then_inc(vd_done[n], 1)

            def trailing(ph, i):
                dve.wait_ge(ph.hi, i + 1)
                u = bank((ph.name, "proj", i))
                for h in range(2):
                    dve.scalar_tensor_tensor(reg(i, "AQ")[HD:2 * HD, h, :], u[HD * h:HD * h + HD, 0, :], HD ** -0.5,
                                             reg(i, "AQ")[0:HD, h, :].bitcast(F32), ALU.mult, ALU.subtract)
                    ins = dve.tensor_tensor(reg(i, "BK")[0:HD, h, 0:ph.NK], u[HD * h:HD * h + HD, 1, 0:ph.NK],
                                            reg(i, "AK")[0:HD, h, 0:ph.NK].bitcast(F32), ALU.subtract)
                ins.then_inc(ph.lo, 1)

            def maxima(ph, i):
                for n in range(ph.smax):
                    m = take()
                    if ph.NC == 4:
                        h, qt = n // TB, n % TB
                        ins = dve.tensor_reduce(mx[:, i % 2, qt, h:h + 1], m[:, :], AX, ALU.max)
                    else:
                        ins = dve.tensor_reduce(mx[:, i % 2, n, :], m[:, 0:2 * S].rearrange("p (h k) -> p h k", h=2),
                                                AX, ALU.max)
                    ins.then_inc(m_free, 1)

            def attention(ph):
                trailing(ph, 0)
                trailing(ph, 1)
                maxima(ph, 0)
                negated(2)
                for i in range(NPAIR + 1):
                    if i + 1 < NPAIR:
                        maxima(ph, i + 1)
                    if i + 2 < NPAIR:
                        trailing(ph, i + 2)
                    if i + 1 < NPAIR:
                        dve.wait_ge(ph.mrow, 32 * (i + 1))
                        negated(2)
                    if i >= 1:
                        dve.wait_ge(ph.rinv, i)
                        b, j = (i - 1) // PAIRS, (i - 1) % PAIRS
                        divide(AT[:, j, b * N:(b + 1) * N], ph.norm)

            def residual(n, name, b):
                dve.wait_ge(o_done[n], b + 1)
                ins = add_row(O, tiles(("o", n), b), name, b)
                ins.then_inc(o_read[n], 1)
                dve.wait_ge(o_read[n], b + 1)
                link(dve.tensor_tensor(X[:, half(b), :], O[:, half(b), :], X[:, half(b), :], ALU.add))
                layernorm(n + 1, X, b)

            values(0, NT, P)
            attention(self_att)
            values(1, 4, SC)
            for b in range(B):
                residual(1, "bo1", b)
            attention(cross_att)
            for b in range(B):
                residual(2, "bo2", b)
            for n in range(B * 4):
                b, m = n // 4, n % 4
                dve.wait_ge(gate_done, n + 1)
                dve.scalar_tensor_tensor(AT[:, m, b * N:(b + 1) * N], bank(("wp", n))[:, 1, :],
                                         cols[:, COL["bp"] + m:COL["bp"] + m + 1], work[:, n % 2, :],
                                         ALU.add, ALU.mult).then_inc(glu_done, 1)
            for b in range(B):
                dve.wait_ge(wf_done, b + 1)
                link(add_row(O, tiles(("wf",), b), "bf", b))
                dve.tensor_tensor(O[:, half(b), :], O[:, half(b), :], X[:, half(b), :], ALU.add).then_inc(y_done, 1)

        @block.tensor
        def _(pe):
            ring = [0]
            seen = set()

            def claim(key):
                k = place[key]
                if k >= 2:
                    pe.wait_ge(*freed[units[k - 2]])
                return ST[k % 2]

            def claim_m():
                k = ring[0]
                ring[0] += 1
                if k >= 2:
                    pe.wait_ge(m_free, k - 1)
                return M[k % 2]

            def loaded(*keys):
                for key in keys:
                    if key not in seen:
                        seen.add(key)
                        pe.wait_ge(ld[key], 16)

            loaded("xT", "wq0")
            for n in range(4):
                u = claim(("q0", n))
                for b in range(B):
                    ins = pe.matmul(u[:, b, :], wq0[:, n, :], xnT[:, b * N:(b + 1) * N], start=True, stop=True)
                ins.then_inc(q0_done, 1)
            loaded("ctxT", "wk0", "wv0")
            for n in range(4, 6):
                u = claim(("q0", n))
                for v in range(2):
                    ins = pe.matmul(u[:, v, 0:B * S], wk0[:, 2 * (n - 4) + v, :], ctxT[:, :], start=True, stop=True)
                ins.then_inc(q0_done, 1)
            u = claim(("v0",))
            for c in range(4):
                ins = pe.matmul(u[0:SC, 0, c * D:(c + 1) * D], ctxT[:, c * SC:(c + 1) * SC], wv0, start=True, stop=True)
            ins.then_inc(v0_done, 1)

            def scores_max0(b, qt):
                for hp in range(H // 2):
                    m = claim_m()
                    for v in range(2):
                        h = 2 * hp + v
                        g, t = h // 4, h % 4
                        q = slice(b * N + qt * P, b * N + (qt + 1) * P)
                        ins = pe.matmul(m[:, v * S:(v + 1) * S], Q0[32 * g:32 * g + 24, t, q],
                                        K0[32 * g:32 * g + 24, t, b * S:(b + 1) * S], start=True, stop=True)
                    ins.then_inc(m_full, 1)

            def turn_maxima(get, n):
                loaded("ident")
                waited = ring[0]
                m = claim_m()
                pe.wait_ge(m_free, waited)
                for qt in range(TB):
                    ins = pe.transpose(m[0:n, qt * P:(qt + 1) * P], get(qt), ident[:, :])
                ins.then_inc(m_full, 1)

            pe.wait_ge(split_done, 6)
            for qt in range(TB):
                scores_max0(0, qt)
            turn_maxima(lambda qt: mx0[:, 0, qt, :], H)
            for i in range(NQUAD + 1):
                if i < NQUAD:
                    b, g = i // 4, i % 4
                    pe.wait_ge(mrow0, 16 * 8 * (b + 1))
                    for j in range(4):
                        u = claim(("s0", i, j))
                        for c in range(2):
                            ins = pe.matmul(u[0:SC, c, :], K0[32 * g:32 * g + 26, j, b * S + c * SC:b * S + (c + 1) * SC],
                                            Q0[32 * g:32 * g + 26, j, b * N:(b + 1) * N], start=True, stop=True)
                        ins.then_inc(st0_done, 1)
                if i < TB:
                    scores_max0(1, i)
                if i == TB - 1:
                    turn_maxima(lambda qt: mx0[:, 1, qt, :], H)
                if i >= 1:
                    k = i - 1
                    pe.wait_ge(exp0_done, 4 * i)
                    if k == 0:
                        pe.wait_ge(v0_ready, 1)
                        pe.wait_ge(ones_set, 1)
                    else:
                        pe.wait_ge(norm0_done, k)
                    b, t = k // 4, k % 4
                    for out_bank, c in ((PV, 0), (PV, 1), (DEN, 0), (DEN, 1)):
                        for j in range(4):
                            w = V0[:, 2 * b + c, 4 * t + j, :] if out_bank is PV else ones[0:SC, 0:32]
                            ins = pe.matmul(out_bank[32 * j:32 * j + 32, :], w, PT0[0:SC, k % 2, j, c, :],
                                            start=(c == 0), stop=(c == 1))
                    ins.then_inc(pv0_done, 1)

            def project_out(key, done, act_tiles, w, n, ready):
                u = claim(key)
                for b in range(B):
                    pe.wait_ge(*ready(b))
                    for t in range(TB):
                        for m in range(n):
                            ins = pe.matmul(u[:, b, t * P:(t + 1) * P], act_tiles[:, m, (TB * b + t) * P:(TB * b + t + 1) * P],
                                            w[:, m, :], start=(m == 0), stop=(m == n - 1))
                    ins.then_inc(done, 1)

            def turn(n):
                u = claim(("t", n))
                for b in range(B):
                    pe.wait_ge(xc_done[n], b + 1)
                    for t in range(TB):
                        ins = pe.transpose(u[:, b, t * P:(t + 1) * P], XC[:, TB * b + t, :], ident[:, :])
                    ins.then_inc(t_done[n], 1)

            loaded("wo0")
            project_out(("o", 0), o_done[0], AT[:, 4:8, :], wo0, 4, lambda b: (norm0_done, 4 * (b + 1)))
            turn(0)
            loaded("w1", "w2")
            for n in range(B * 2):
                b = n // 2
                pe.wait_ge(xn_done[0], b + 1)
                u = claim(("w1", n))
                for mm in range(2):
                    m = 2 * (n % 2) + mm
                    ins = pe.matmul(u[:, mm, :], w1[:, m * P:(m + 1) * P], xnT[:, b * N:(b + 1) * N], start=True, stop=True)
                ins.then_inc(w1_done, 1)
            project_out(("w2",), w2_done, AT, w2, 4, lambda b: (gelu_done, 4 * (b + 1)))
            turn(1)

            def values(n, tiles, r, src, w, ready):
                for t in range(tiles):
                    ready(t)
                    u = claim(("v", n, t))
                    for v in range(2):
                        ins = pe.matmul(u[0:r, v, :], src[:, t * r:(t + 1) * r], w[:, v * N:(v + 1) * N], start=True, stop=True)
                    ins.then_inc(v_done[n], 1)

            def project(ph, i, wk, src):
                u = claim((ph.name, "proj", i))
                b, j = i // PAIRS, i % PAIRS
                pe.matmul(u[:, 0, :], Wq[:, j * P:(j + 1) * P], xnT[:, b * N:(b + 1) * N], start=True, stop=True)
                pe.matmul(u[:, 1, 0:ph.NK], wk[:, j * P:(j + 1) * P], src[:, b * ph.NK:(b + 1) * ph.NK],
                          start=True, stop=True).then_inc(ph.proj, 1)

            def scores_max(ph, i, n):
                m = claim_m()
                if n == 0:
                    pe.wait_ge(ph.lo, i + 1)
                heads = [(n // TB, 0)] if ph.NC == 4 else [(0, 0), (1, S)]
                for h, at in heads:
                    ins = pe.matmul(m[:, at:at + ph.NK], reg(i, "AQ")[:, h, (n % TB) * P:(n % TB + 1) * P],
                                    reg(i, "AK")[:, h, 0:ph.NK], start=True, stop=True)
                ins.then_inc(m_full, 1)

            def scores(ph, i):
                pe.wait_ge(ph.mrow, 32 * (i + 1))
                per = ph.units // 2
                for n in range(ph.units):
                    u = claim((ph.name, "st", i, n))
                    h = n // per
                    for v in range(2):
                        c = 2 * (n % per) + v
                        k = slice(c * ph.KC, (c + 1) * ph.KC)
                        pe.matmul(u[0:ph.KC, v, :], reg(i, "AK")[:, h, k], reg(i, "AQ")[:, h, :], start=True, stop=False)
                        ins = pe.matmul(u[0:ph.KC, v, :], reg(i, "BK")[:, h, k], reg(i, "BQ")[:, h, :],
                                        start=False, stop=True)
                    ins.then_inc(ph.st, 1)

            def attention(ph, wk, src):
                project(ph, 0, wk, src)
                project(ph, 1, wk, src)
                for n in range(ph.smax):
                    scores_max(ph, 0, n)
                turn_maxima(lambda qt: mx[:, 0, qt, :], 2)
                for i in range(NPAIR + 1):
                    if i + 2 < NPAIR:
                        project(ph, i + 2, wk, src)
                    if i >= 1:
                        k = i - 1
                        pe.wait_ge(ph.exp, ph.units * i)
                        if k >= 1:
                            pe.wait_ge(ph.pvs, k)
                    for c in range(ph.NC):
                        if i >= 1:
                            b, j = k // PAIRS, k % PAIRS
                            for h in range(2):
                                ins = pe.matmul(PV[HD * h:HD * (h + 1), :],
                                                V[0:ph.KC, b * ph.NC + c, (2 * j + h) * HD:(2 * j + h + 1) * HD],
                                                PT1[0:ph.KC, k % 2, h, c, :], start=(c == 0), stop=(c == ph.NC - 1))
                            if c == ph.NC - 1:
                                ins.then_inc(ph.pv, 1)
                        if i + 1 < NPAIR:
                            for n in range(2):
                                scores_max(ph, i + 1, 2 * c + n)
                    if i >= 1:
                        pe.wait_ge(ph.sum, i)
                        if i >= 2:
                            pe.wait_ge(ph.norm, i - 1)
                        for h in range(2):
                            ins = pe.matmul(DEN[HD * h:HD * (h + 1), :], ones[0:ph.KC, :], psums[0:ph.KC, h, :],
                                            start=True, stop=True)
                        ins.then_inc(ph.den, 1)
                    if i < NPAIR:
                        scores(ph, i)
                    if i + 1 < NPAIR:
                        turn_maxima(lambda qt: mx[:, (i + 1) % 2, qt, :], 2)

            loaded("wv1", "wq1", "wk1", "wo1")
            values(0, NT, P, xnT, Wv, lambda t: pe.wait_ge(xn_done[1], t // TB + 1))
            pe.wait_ge(kones_set, 1)
            pe.wait_ge(va_done[0], NT // 2)
            pe.wait_ge(vd_done[0], NT // 2)
            attention(self_att, Wk, xnT)
            loaded("wv2")
            values(1, 4, SC, ctxT, Wv[0:C, :], lambda t: None)
            project_out(("o", 1), o_done[1], AT, Wo, PAIRS, lambda b: (self_att.norm, PAIRS * (b + 1)))
            loaded("wq2", "wk2")
            turn(2)
            pe.wait_ge(xn_done[2], B)
            pe.wait_ge(va_done[1], 2)
            pe.wait_ge(vd_done[1], 2)
            attention(cross_att, Wk[0:C, :], ctxT)
            loaded("wo2", "wp", "wf")
            project_out(("o", 2), o_done[2], AT, Wo, PAIRS, lambda b: (cross_att.norm, PAIRS * (b + 1)))
            turn(3)
            for n in range(B * 4):
                b, m = n // 4, n % 4
                pe.wait_ge(xn_done[3], b + 1)
                u = claim(("wp", n))
                pe.matmul(u[:, 0, :], wp[:, FF + m * P:FF + (m + 1) * P], xnT[:, b * N:(b + 1) * N], start=True, stop=True)
                pe.matmul(u[:, 1, :], wp[:, m * P:(m + 1) * P], xnT[:, b * N:(b + 1) * N],
                          start=True, stop=True).then_inc(wp_done, 1)
            project_out(("wf",), wf_done, AT, wf, 4, lambda b: (glu_done, 4 * (b + 1)))


def kernel(**inputs):
    import numpy as np
    import concourse.bacc as bacc
    from concourse.bass_utils import run_bass_kernel_spmd

    def get(name):
        return np.ascontiguousarray(inputs[name])

    def bands(w):
        k = w.shape[0]
        heads = w.reshape(k, 4, 4, HD0)
        tiles = np.zeros((k, 4, 4, 32), w.dtype)
        for r in range(3):
            tiles[:, :, :, HD0 * r:HD0 * (r + 1)] = heads.transpose(0, 2, 1, 3)
        return tiles.reshape(k, 4, P)

    x, ctx = get("x"), get("ctx_768")
    cols = np.zeros((P, NCOL), x.dtype)
    cols[:, 0:4] = bands(get("L0_xattn_bq")[None])[0].T
    cols[:, 4:8] = bands(get("L0_xattn_bk")[None])[0].T
    for g in range(4):
        cols[32 * g + 24:32 * g + 26, 4:8] = 1
        cols[32 * g + 16:32 * g + 24, COL["nq0"]] = -1
        cols[32 * g + 8:32 * g + 16, COL["nk0"]] = -1
    for key, name in (("ln_g", "L0_xattn_ln_g"), ("ln_b", "L0_xattn_ln_b"), ("g1", "L1_xattn_g1"), ("c1", "L1_xattn_b1"),
                      ("g2", "L1_xattn_g2"), ("c2", "L1_xattn_b2"), ("g3", "L1_xattn_g3"), ("c3", "L1_xattn_b3")):
        cols[:, COL[key]] = get(name)
    cols[:, COL["b1"]:COL["b1"] + 4] = get("L0_xattn_b1").reshape(4, P).T
    cols[:, COL["bp"]:COL["bp"] + 8] = get("L1_xattn_bp").reshape(8, P).T
    rows = np.stack([get(n) for n in ("L0_xattn_bv", "L0_xattn_bo", "L0_xattn_b2", "L1_xattn_bo1", "L1_xattn_bo2", "L1_xattn_bf")])
    wo0 = np.zeros((4, 32, 4, D), x.dtype)
    wo0[:, 0:HD0] = get("L0_xattn_Wo").reshape(4, 4, HD0, D).transpose(1, 2, 0, 3)
    arrays = {
        "x": x, "xT": x.reshape(B * N, D).T, "ctxT": ctx.reshape(B * S, C).T,
        "wq0": bands(get("L0_xattn_Wq")), "wk0": bands(get("L0_xattn_Wk")), "wv0": get("L0_xattn_Wv"),
        "wo0": wo0.reshape(P, 4, D), "w1": get("L0_xattn_W1"), "w2": get("L0_xattn_W2"),
        "wq1": get("L1_xattn_Wq1"), "wk1": get("L1_xattn_Wk1"), "wv1": get("L1_xattn_Wv1"), "wo1": get("L1_xattn_Wo1"),
        "wq2": get("L1_xattn_Wq2"), "wk2": get("L1_xattn_Wk2"), "wv2": get("L1_xattn_Wv2"), "wo2": get("L1_xattn_Wo2"),
        "wp": get("L1_xattn_Wp"), "wf": get("L1_xattn_Wf"), "cols": cols,
        "rows": np.broadcast_to(rows, (P,) + rows.shape), "ident": np.eye(P, dtype=x.dtype),
    }
    nc = bacc.Bacc("TRN2", target_bir_lowering=False, num_devices=1)
    feed, args = {}, {}
    for name, array in arrays.items():
        array = np.ascontiguousarray(array)
        feed[f"in_{name}"] = array
        args[name] = nc.dram_tensor(f"in_{name}", array.shape, mybir.dt.from_np(array.dtype), kind="ExternalInput").ap()
    out = nc.dram_tensor("out_y", (B, N, D), F32, kind="ExternalOutput").ap()
    build(nc, args, out)
    result = run_bass_kernel_spmd(nc, [feed], core_ids=[0])
    return result.results[0]["out_y"]
```
